# Optimizing a Trainium2 kernel written in Bass

```python
import numpy as np
import jax
import jax.numpy as jnp

def _softmax(x, axis=-1):
    return jax.nn.softmax(x, axis=axis)

def _gelu(x):
    return jax.nn.gelu(x, approximate=True)

def _silu(x):
    return jax.nn.silu(x)

def _sigmoid(x):
    return jax.nn.sigmoid(x)

def _layernorm(x, axis=-1, eps=1e-05):
    m = jnp.mean(x, axis=axis, keepdims=True)
    v = jnp.var(x, axis=axis, keepdims=True)
    return (x - m) / jnp.sqrt(v + eps)

def _scatter_add(tgt, idx, src, axis=0):
    return tgt.at[idx].add(src)

def _segment_sum(src, seg, n):
    return jax.ops.segment_sum(src, seg, n)
kernel_name = 'mk_flamingo_gated_d2_seqx_r4_2b5f93'

def setup_inputs(seed: int=0):
    np.random.seed(seed)
    _w = jnp.asarray

    def _rec_inputs():
        import jax
        import jax.numpy as jnp
        _rk = jax.random.key(seed)
        x = -0.000125 + 0.9999 * jax.random.normal(jax.random.fold_in(_rk, 1), (4, 512, 512), jnp.float32)
        _lenS = 512 - jax.random.randint(jax.random.fold_in(_rk, 7), (4,), 0, max(1, 512 // 4) + 1, jnp.int32)
        _lenS2 = 512 - jax.random.randint(jax.random.fold_in(_rk, 8), (4,), 0, max(1, 512 // 4) + 1, jnp.int32)
        fside_BxS2xS2_0 = -3.05549e-07 + 0.0199987 * jax.random.normal(jax.random.fold_in(_rk, 11), (4, 512, 512), jnp.float32)
        _ctx_1024P = jax.random.normal(jax.random.fold_in(_rk, 12), (4, 16, 256), jnp.float32)
        _ctx_1024c = jax.random.dirichlet(jax.random.fold_in(_rk, 512), 0.3 * jnp.ones((16,), jnp.float32), (4, 512))
        _ctx_1024t = jnp.einsum('bsk,bkd->bsd', _ctx_1024c, _ctx_1024P)
        _ctx_1024t = _ctx_1024t * jax.lax.rsqrt(jnp.mean(jnp.square(_ctx_1024t)) + 1e-12) * 0.953939
        ctx_1024 = 6.82029e-06 + 0.0200006 * (_ctx_1024t + 0.3 * jax.random.normal(jax.random.fold_in(_rk, 612), (4, 512, 256), jnp.float32))
        _g = jax.random.normal(jax.random.fold_in(_rk, 9001), (2, 2), jnp.float32)
        _g = jnp.sign(_g) * jnp.maximum(jnp.abs(_g), 1.0) + (_g == 0) * 1.0
        g_xattn = _g[0]
        g_ffn = _g[1]
        return (x, fside_BxS2xS2_0, ctx_1024, g_xattn, g_ffn)
    x, fside_BxS2xS2_0, ctx_1024, g_xattn, g_ffn = _rec_inputs()

    def _L0_xattn_setup():
        import jax, jax.numpy as jnp
        import numpy as np
        EPS = 1e-06
        QMAX = 127.0

        def _smooth_quant_linear(x, w):
            amax_x = jnp.max(jnp.abs(x), axis=0)
            amax_w = jnp.max(jnp.abs(w), axis=0)
            s = jnp.sqrt(jnp.maximum(amax_x, EPS) / jnp.maximum(amax_w, EPS))
            s = jnp.maximum(s, EPS)
            xs = x / s
            ws = w * s
            x_scale = jnp.maximum(jnp.max(jnp.abs(xs), axis=-1, keepdims=True), EPS) / QMAX
            w_scale = jnp.maximum(jnp.max(jnp.abs(ws), axis=-1, keepdims=True), EPS) / QMAX
            x_q = jnp.clip(jnp.round(xs / x_scale), -QMAX, QMAX)
            w_q = jnp.clip(jnp.round(ws / w_scale), -QMAX, QMAX)
            return x_q @ w_q.T * x_scale * w_scale.T

        def _expert_forward(xe, guw, dw):
            h = _smooth_quant_linear(xe, guw)
            gate, up = jnp.split(h, 2, axis=-1)
            a = jax.nn.silu(gate) * up
            return _smooth_quant_linear(a, dw)
        key = jax.random.key(seed)
        k1, k2, k3 = jax.random.split(key, 3)
        E, T, D, I = (8, 512, 512, 256)
        x = jax.random.normal(k1, (E, T, D), dtype=jnp.float32)
        gate_up_weight = jax.random.normal(k2, (E, 2 * I, D), dtype=jnp.float32) * 0.02
        down_weight = jax.random.normal(k3, (E, D, I), dtype=jnp.float32) * 0.02
        return {'x': x, 'gate_up_weight': gate_up_weight, 'down_weight': down_weight}
    _L0_xattn_all = _L0_xattn_setup()
    _L0_xattn_in = {k: v for k, v in _L0_xattn_all.items() if k in ()}
    del _L0_xattn_all

    def _L0_ffn_setup():
        import jax, jax.numpy as jnp
        import numpy as np

        def fwht(x):
            n = x.shape[-1]
            orig_shape = x.shape
            x = x.reshape(-1, n)
            h = 1
            while h < n:
                x = x.reshape(-1, n // (2 * h), 2, h)
                a = x[:, :, 0, :]
                b = x[:, :, 1, :]
                x = jnp.stack([a + b, a - b], axis=2)
                h *= 2
            x = x.reshape(orig_shape)
            return x * (1.0 / jnp.sqrt(jnp.asarray(n, dtype=x.dtype)))

        def act_quant(x, bits):
            qb = 2.0 ** (bits - 1) - 1.0
            scale = qb / jnp.clip(jnp.max(jnp.abs(x), axis=-1, keepdims=True), 1e-05, None)
            q = jnp.clip(jnp.round(x * scale), -qb, qb) / scale
            return x + jax.lax.stop_gradient(q - x)

        def weight_quant(w):
            scale = jnp.clip(jnp.mean(jnp.abs(w)), 1e-05, None)
            q = jnp.clip(jnp.round(w / scale), -1.0, 1.0) * scale
            return w + jax.lax.stop_gradient(q - w)

        def hbitlinear(x, w, bits):
            xh = fwht(x)
            xq = act_quant(xh, bits)
            wq = weight_quant(w)
            return jnp.einsum('bsh,oh->bso', xq, wq)
        key = jax.random.key(seed)
        k1, k2, k3 = jax.random.split(key, 3)
        B, S, H = (4, 512, 512)
        I = 1024
        hidden_states = jax.random.normal(k1, (B, S, H), dtype=jnp.float32)
        w_up = jax.random.normal(k2, (I, H), dtype=jnp.float32) * 0.02
        w_down = jax.random.normal(k3, (H, I), dtype=jnp.float32) * 0.02
        return {'hidden_states': hidden_states, 'w_up': w_up, 'w_down': w_down}
    _L0_ffn_all = _L0_ffn_setup()
    _L0_ffn_in = {k: v for k, v in _L0_ffn_all.items() if k in ('w_up', 'w_down')}
    del _L0_ffn_all

    def _L1_xattn_setup():
        import jax, jax.numpy as jnp
        import numpy as np
        key = jax.random.key(seed)
        ks = jax.random.split(key, 6)
        B, L, N, C, D = (8, 128, 512, 256, 128)
        return {'teacher_logits': jax.random.normal(ks[0], (B, L, N), dtype=jnp.float32), 'teacher_features': jax.random.normal(ks[1], (B, N, C), dtype=jnp.float32), 'Wq': jax.random.normal(ks[2], (D, C), dtype=jnp.float32) * (1.0 / np.sqrt(C)), 'bq': jnp.zeros((D,), dtype=jnp.float32), 'Wk': jax.random.normal(ks[3], (D, C), dtype=jnp.float32) * (1.0 / np.sqrt(C)), 'bk': jnp.zeros((D,), dtype=jnp.float32)}
    _L1_xattn_all = _L1_xattn_setup()
    _L1_xattn_in = {k: v for k, v in _L1_xattn_all.items() if k in ('Wq', 'bq', 'Wk', 'bk')}
    del _L1_xattn_all

    def _L1_ffn_setup():
        import jax, jax.numpy as jnp
        import numpy as np
        B, S, H = (2, 512, 512)
        E, K, F = (32, 4, 352)
        FS = 1408
        EPS = 1e-06
        CAP = 256
        key = jax.random.key(seed)
        ks = jax.random.split(key, 10)
        s = 0.02
        return {'hidden_states': jax.random.normal(ks[0], (B, S, H), jnp.float32), 'w_norm': 1.0 + 0.02 * jax.random.normal(ks[1], (H,), jnp.float32), 'w_router': s * jax.random.normal(ks[2], (H, E), jnp.float32), 'w_gate': s * jax.random.normal(ks[3], (E, H, F), jnp.float32), 'w_up': s * jax.random.normal(ks[4], (E, H, F), jnp.float32), 'w_down': s * jax.random.normal(ks[5], (E, F, H), jnp.float32), 'sw_gate': s * jax.random.normal(ks[6], (H, FS), jnp.float32), 'sw_up': s * jax.random.normal(ks[7], (H, FS), jnp.float32), 'sw_down': s * jax.random.normal(ks[8], (FS, H), jnp.float32), 'w_shared_gate': s * jax.random.normal(ks[9], (H, 1), jnp.float32)}
    _L1_ffn_all = _L1_ffn_setup()
    _L1_ffn_in = {k: v for k, v in _L1_ffn_all.items() if k in ('w_norm', 'w_router', 'w_gate', 'w_up', 'w_down', 'sw_gate', 'sw_up', 'sw_down', 'w_shared_gate')}
    del _L1_ffn_all
    return {'x': x, 'fside_BxS2xS2_0': fside_BxS2xS2_0, 'ctx_1024': ctx_1024, 'g_xattn': g_xattn, 'g_ffn': g_ffn, 'L0_ffn_w_up': _L0_ffn_in['w_up'], 'L0_ffn_w_down': _L0_ffn_in['w_down'], 'L1_xattn_Wq': _L1_xattn_in['Wq'], 'L1_xattn_bq': _L1_xattn_in['bq'], 'L1_xattn_Wk': _L1_xattn_in['Wk'], 'L1_xattn_bk': _L1_xattn_in['bk'], 'L1_ffn_w_norm': _L1_ffn_in['w_norm'], 'L1_ffn_w_router': _L1_ffn_in['w_router'], 'L1_ffn_w_gate': _L1_ffn_in['w_gate'], 'L1_ffn_w_up': _L1_ffn_in['w_up'], 'L1_ffn_w_down': _L1_ffn_in['w_down'], 'L1_ffn_sw_gate': _L1_ffn_in['sw_gate'], 'L1_ffn_sw_up': _L1_ffn_in['sw_up'], 'L1_ffn_sw_down': _L1_ffn_in['sw_down'], 'L1_ffn_w_shared_gate': _L1_ffn_in['w_shared_gate']}

def reference(x, fside_BxS2xS2_0, ctx_1024, g_xattn, g_ffn, L0_ffn_w_up, L0_ffn_w_down, L1_xattn_Wq, L1_xattn_bq, L1_xattn_Wk, L1_xattn_bk, L1_ffn_w_norm, L1_ffn_w_router, L1_ffn_w_gate, L1_ffn_w_up, L1_ffn_w_down, L1_ffn_sw_gate, L1_ffn_sw_up, L1_ffn_sw_down, L1_ffn_w_shared_gate):
    import jax
    import jax.numpy as jnp

    def _L0_xattn_ref(x, gate_up_weight, down_weight):
        import jax, jax.numpy as jnp
        import numpy as np
        EPS = 1e-06
        QMAX = 127.0

        def _smooth_quant_linear(x, w):
            amax_x = jnp.max(jnp.abs(x), axis=0)
            amax_w = jnp.max(jnp.abs(w), axis=0)
            s = jnp.sqrt(jnp.maximum(amax_x, EPS) / jnp.maximum(amax_w, EPS))
            s = jnp.maximum(s, EPS)
            xs = x / s
            ws = w * s
            x_scale = jnp.maximum(jnp.max(jnp.abs(xs), axis=-1, keepdims=True), EPS) / QMAX
            w_scale = jnp.maximum(jnp.max(jnp.abs(ws), axis=-1, keepdims=True), EPS) / QMAX
            x_q = jnp.clip(jnp.round(xs / x_scale), -QMAX, QMAX)
            w_q = jnp.clip(jnp.round(ws / w_scale), -QMAX, QMAX)
            return x_q @ w_q.T * x_scale * w_scale.T

        def _expert_forward(xe, guw, dw):
            h = _smooth_quant_linear(xe, guw)
            gate, up = jnp.split(h, 2, axis=-1)
            a = jax.nn.silu(gate) * up
            return _smooth_quant_linear(a, dw)
        return jax.vmap(_expert_forward)(x, gate_up_weight, down_weight)

    def _L0_ffn_ref(hidden_states, w_up, w_down):
        import jax, jax.numpy as jnp
        import numpy as np

        def fwht(x):
            n = x.shape[-1]
            orig_shape = x.shape
            x = x.reshape(-1, n)
            h = 1
            while h < n:
                x = x.reshape(-1, n // (2 * h), 2, h)
                a = x[:, :, 0, :]
                b = x[:, :, 1, :]
                x = jnp.stack([a + b, a - b], axis=2)
                h *= 2
            x = x.reshape(orig_shape)
            return x * (1.0 / jnp.sqrt(jnp.asarray(n, dtype=x.dtype)))

        def act_quant(x, bits):
            qb = 2.0 ** (bits - 1) - 1.0
            scale = qb / jnp.clip(jnp.max(jnp.abs(x), axis=-1, keepdims=True), 1e-05, None)
            q = jnp.clip(jnp.round(x * scale), -qb, qb) / scale
            return x + jax.lax.stop_gradient(q - x)

        def weight_quant(w):
            scale = jnp.clip(jnp.mean(jnp.abs(w)), 1e-05, None)
            q = jnp.clip(jnp.round(w / scale), -1.0, 1.0) * scale
            return w + jax.lax.stop_gradient(q - w)

        def hbitlinear(x, w, bits):
            xh = fwht(x)
            xq = act_quant(xh, bits)
            wq = weight_quant(w)
            return jnp.einsum('bsh,oh->bso', xq, wq)
        ACT_BITS = 8
        h = hbitlinear(hidden_states, w_up, ACT_BITS)
        h = jnp.square(jax.nn.relu(h))
        out = hbitlinear(h, w_down, ACT_BITS)
        return out

    def _L1_xattn_ref(teacher_logits, teacher_features, Wq, bq, Wk, bk):
        import jax, jax.numpy as jnp
        import numpy as np
        query = jnp.einsum('bnc,dc->bnd', teacher_features, Wq) + bq
        key = jnp.einsum('bnc,dc->bnd', teacher_features, Wk) + bk
        energy = jnp.einsum('bnd,bmd->bnm', query, key)
        attention = jax.nn.softmax(energy, axis=-1)
        x_m = jnp.einsum('bln,bmn->blm', teacher_logits, attention)
        return x_m

    def _L1_ffn_ref(hidden_states, w_norm, w_router, w_gate, w_up, w_down, sw_gate, sw_up, sw_down, w_shared_gate):
        import jax, jax.numpy as jnp
        import numpy as np
        B, S, H = (2, 512, 512)
        E, K, F = (32, 4, 352)
        FS = 1408
        EPS = 1e-06
        CAP = 256
        inp = hidden_states
        xf = inp.astype(jnp.float32)
        var = jnp.mean(xf * xf, axis=-1, keepdims=True)
        x = (w_norm * (xf * jax.lax.rsqrt(var + EPS))).astype(inp.dtype)
        Bq, Sq, Hq = x.shape
        x = x.reshape(-1, Hq)
        T = Bq * Sq
        logits = x @ w_router
        probs = jax.nn.softmax(logits.astype(jnp.float32), axis=-1)
        w_topk, sel = jax.lax.top_k(probs, K)
        w_topk = w_topk.astype(x.dtype)
        flat_e = sel.reshape(-1)
        order = jnp.argsort(flat_e)
        sorted_e = flat_e[order]
        counts = jnp.zeros((E,), jnp.int32).at[flat_e].add(1)
        starts = jnp.cumsum(counts) - counts
        pos = jnp.arange(T * K) - starts[sorted_e]
        tok = order // K
        valid = pos < CAP
        dest = jnp.where(valid, pos, CAP)
        buf = jnp.zeros((E, CAP + 1, Hq), x.dtype).at[sorted_e, dest].set(x[tok])
        buf = buf[:, :CAP]
        g = jnp.einsum('ech,ehf->ecf', buf, w_gate)
        u = jnp.einsum('ech,ehf->ecf', buf, w_up)
        y = jnp.einsum('ecf,efh->ech', jax.nn.silu(g) * u, w_down)
        wv = w_topk.reshape(-1)[order] * valid.astype(x.dtype)
        gath = y[sorted_e, jnp.minimum(pos, CAP - 1)]
        out = jnp.zeros((T, Hq), x.dtype).at[tok].add(gath * wv[:, None])
        sh = jax.nn.silu(x @ sw_gate) * (x @ sw_up) @ sw_down
        sh = jax.nn.sigmoid(x @ w_shared_gate) * sh
        out = out + sh
        return inp + out.reshape(Bq, Sq, Hq)
    x = x + jnp.tanh(g_xattn[0]) * _L0_xattn_ref(_layernorm(x, axis=-1), fside_BxS2xS2_0, ctx_1024)
    x = x + jnp.tanh(g_ffn[0]) * _L0_ffn_ref(_layernorm(x, axis=-1), L0_ffn_w_up, L0_ffn_w_down)
    x = x + jnp.tanh(g_xattn[1]) * _L1_xattn_ref(_layernorm(x, axis=-1), ctx_1024, L1_xattn_Wq, L1_xattn_bq, L1_xattn_Wk, L1_xattn_bk)
    x = x + jnp.tanh(g_ffn[1]) * _L1_ffn_ref(_layernorm(x, axis=-1), L1_ffn_w_norm, L1_ffn_w_router, L1_ffn_w_gate, L1_ffn_w_up, L1_ffn_w_down, L1_ffn_sw_gate, L1_ffn_sw_up, L1_ffn_sw_down, L1_ffn_w_shared_gate)
    return x

_drawn_inputs = setup_inputs


def setup_inputs(seed=0):
    import zlib

    import numpy as np

    out = dict(_drawn_inputs(seed))
    spreads = {'g_ffn': (-1.0, 0.2), 'L1_xattn_bq': (0.0, 0.8), 'L1_xattn_bk': (0.0, 0.8)}
    factors = {'L1_xattn_Wq': 8.0,
     'L1_xattn_Wk': 8.0,
     'L1_ffn_w_norm': 8.0,
     'L1_ffn_w_router': 2.804,
     'L1_ffn_w_gate': 2.68}
    for name, (base, spread) in spreads.items():
        noise = np.random.default_rng([zlib.crc32(name.encode()), seed]).standard_normal(out[name].shape)
        drawn = base * np.exp(spread * noise) if base else spread * noise
        out[name] = jnp.asarray(drawn.astype(out[name].dtype))
    for name, factor in factors.items():
        out[name] = (out[name] * factor).astype(out[name].dtype)
    return out
```

```python
from contextlib import ExitStack

import concourse.bass as bass
from concourse import mybir

F32 = mybir.dt.float32
BF16 = mybir.dt.bfloat16
U32 = mybir.dt.uint32
ALU = mybir.AluOpType
ACT = mybir.ActivationFunctionType
AX = mybir.AxisListType

P = 128
BATCH, SEQ, D = 4, 512, 512
TPB = SEQ // P
NT = BATCH * TPB
DC = D // P
IA = 256
IB = 1024
IBC = IB // P
CTX = 256
CC = CTX // P
E, TOPK, F, CAP = 32, 4, 352, 256
FS = 1408
FSC = FS // P
FCH = [(0, 128), (128, 128), (256, 96)]
SLOTS = E * CAP
MAGIC = 12582912.0
TAB = 3 * P + E + 1 + NT * TOPK
TINY = 1e-6


def flamingo_block(nc, x, fside, ctx, g_xattn, g_ffn, wupT, wdownT, WqT, bq, WkT, bk, w_norm, w_router,
                   w_gate, w_up, w_down, sw_gate, sw_up, sw_down, w_sgate, ctxT, const_tab, const_had, out):
    dispatched = nc.dram_tensor("dispatched_rows", [SLOTS + NT * P * TOPK, D], F32, kind="Internal").ap()
    expert_out = nc.dram_tensor("expert_rows", [SLOTS, D], F32, kind="Internal").ap()

    with ExitStack() as stack:
        def sb(name, shape, dt):
            return stack.enter_context(nc.sbuf_tensor(name, shape, dt))

        def sem(name):
            return stack.enter_context(nc.semaphore(name))

        X = sb("X", [P, NT * D], F32)
        XR = sb("XR", [P, NT * D], F32)
        XRT = sb("XRT", [P, DC, NT * P], F32)
        tab = sb("tab", [P, TAB], F32)
        identb = sb("identb", [P, P], BF16)
        arena = sb("arena", [P, 27136], F32)
        small = sb("small", [P, 640], F32)
        small_u = sb("small_u", [P, 2 * NT * TOPK], U32)

        def part(at, n):
            return arena[:, at:at + n]

        ident = tab[:, 0:P]
        tri = tab[:, P:2 * P]
        ones = tab[:, 2 * P:3 * P]
        iota = tab[:, 3 * P:3 * P + E]
        magic = tab[:, 3 * P + E:3 * P + E + 1]
        spare = tab[:, 3 * P + E + 1:TAB].rearrange("p (t k) -> p t k", k=TOPK)
        had = XRT[:, :, :].rearrange("p a b -> p (a b)")

        cursor = [0]

        def scal(n):
            cursor[0] += n
            assert cursor[0] <= 640
            return small[:, cursor[0] - n:cursor[0]]

        bank = [stack.enter_context(nc.psum_tensor(f"bank{i}", [P, 512], F32)) for i in range(8)]
        bankb = [b[:, :].bitcast(BF16) for b in bank]

        const_in = sem("const_in")
        x_in = sem("x_in")
        ident_ready = sem("ident_ready")
        passed = {n: sem("passed_" + n) for n in ("pe", "act", "dve", "pool", "sp")}
        tanh_ready = sem("tanh_ready")
        var_ready = sem("var_ready")
        root_ready = sem("root_ready")
        fside_in = [sem(f"fside_in{s}") for s in range(2)]
        ctx_in = [sem(f"ctx_in{s}") for s in range(2)]
        a_used = sem("a_used")
        q_fold = sem("q_fold")
        q_foldT = sem("q_foldT")
        q_ratio = sem("q_ratio")
        q_root = sem("q_root")
        q_s = sem("q_s")
        q_bc = sem("q_bc")
        q_inv = sem("q_inv")
        q_magic = sem("q_magic")
        q_int = sem("q_int")
        q_intT = sem("q_intT")
        q_lhs = sem("q_lhs")
        q_wbc = sem("q_wbc")
        q_mm = sem("q_mm")
        a_out = sem("a_out")
        a_h = sem("a_h")
        a_silu = sem("a_silu")
        wb_in = sem("wb_in")
        had_in = sem("had_in")
        wb_sum = sem("wb_sum")
        wb_tot = sem("wb_tot")
        b_xn = sem("b_xn")
        b_xnT = sem("b_xnT")
        b_xnTs = sem("b_xnTs")
        b_rot = sem("b_rot")
        b_inv = sem("b_inv")
        b_magic = sem("b_magic")
        b_int = sem("b_int")
        b_intT = sem("b_intT")
        b_q = sem("b_q")
        b_up = sem("b_up")
        b_relu = sem("b_relu")
        b_sq = sem("b_sq")
        b_down = sem("b_down")
        b_done = sem("b_done")
        wc_in = sem("wc_in")
        ctxT_in = sem("ctxT_in")
        c_proj = sem("c_proj")
        c_qk = sem("c_qk")
        c_energy = sem("c_energy")
        c_max = sem("c_max")
        c_exp = sem("c_exp")
        c_prob = sem("c_prob")
        c_probT = sem("c_probT")
        c_pT = sem("c_pT")
        c_xn = sem("c_xn")
        c_xnT = sem("c_xnT")
        c_xT = sem("c_xT")
        c_mix = sem("c_mix")
        c_done = sem("c_done")
        router_in = sem("router_in")
        shared_in = sem("shared_in")
        zeroed = sem("zeroed")
        rows_cleared = sem("rows_cleared")
        ms_ready = sem("ms_ready")
        rms_ready = sem("rms_ready")
        d_xr = sem("d_xr")
        d_xrT = sem("d_xrT")
        d_xT = sem("d_xT")
        d_logit = sem("d_logit")
        r_shift = sem("r_shift")
        r_exp = sem("r_exp")
        r_mask = sem("r_mask")
        r_rank = sem("r_rank")
        r_index = sem("r_index")
        scattered = sem("scattered")
        s_gu = sem("s_gu")
        s_silu = sem("s_silu")
        s_h = sem("s_h")
        s_out = sem("s_out")
        s_added = sem("s_added")
        ew_in = [sem(f"ew_in{s}") for s in range(2)]
        e_rowsT = sem("e_rowsT")
        e_xT = sem("e_xT")
        e_gu = sem("e_gu")
        e_silu = sem("e_silu")
        e_h = sem("e_h")
        e_down = sem("e_down")
        e_y = sem("e_y")
        y_out = [sem(f"y_out{s}") for s in range(2)]
        gathered = [sem(f"gathered{s}") for s in range(4)]
        combined = sem("combined")
        final_out = sem("final_out")

        def wait(eng, who, signal, value):
            eng.wait_ge(signal, value)
            eng.sem_inc(passed[who], 1)

        def xtile(T):
            return X[:, bass.ds(T * D, D)] if not isinstance(T, int) else X[:, T * D:(T + 1) * D]

        gates = scal(4)
        tg = scal(4)
        bn = scal(6 * TPB)
        mv = scal(2 * TPB)
        veps = scal(TPB)
        rstd = scal(TPB)
        ms = scal(TPB)
        rms = scal(TPB)
        maxs = scal(8)
        lim = scal(8)
        ratio = scal(4)
        root = scal(4)
        s_col = scal(4)
        rs_col = scal(4)
        rowmax = scal(8)
        rowscale = scal(8)
        rowinv = scal(8)
        gscale = scal(4)
        wsum = scal(2)
        wscale = scal(2)
        winv = scal(2)
        bs = scal(8 * TPB)
        negmax = scal(TPB)
        esum = scal(TPB)
        ersum = scal(TPB)
        bias_qk = scal(2)
        sgate = scal(NT)
        sg_e = scal(NT)
        choice_w = scal(NT * TOPK)
        rmax = scal(NT)
        rsum = scal(NT)
        phalf = scal(4)
        mhalf4 = scal(4)
        scatter_at = small_u[:, 0:NT * TOPK]
        gather_at = small_u[:, NT * TOPK:2 * NT * TOPK]

        fs_buf = [part(2048 * s, 2048).rearrange("p (t c) -> p t c", t=TPB) for s in range(2)]
        cx_buf = [part(4096 + 1024 * s, 1024).rearrange("p (t c) -> p t c", t=TPB) for s in range(2)]
        xnA = part(6144, 2048).rearrange("p (t c) -> p t c", t=TPB)
        scaled = part(8192, 4096).rearrange("p (t c) -> p t c", t=8)
        ints = part(12288, 2048).bitcast(BF16).rearrange("p (t c) -> p t c", t=8)
        intsT = part(14336, 2048).bitcast(BF16).rearrange("p (j t) -> p j t", j=DC)
        hA = part(16384, 2048).rearrange("p (t c) -> p t c", t=TPB)
        actA = part(18432, 1024).rearrange("p (t c) -> p t c", t=TPB)
        fold = part(19456, 3072).rearrange("p (w k c) -> p w k c", w=2, k=3)
        wupR = XR[:, 0:DC * IB]
        wdownR = XR[:, DC * IB:DC * IB + IBC * D]
        wupQ = part(22528, 2048).bitcast(BF16).rearrange("p (j o) -> p j o", j=DC)
        wdownQ = part(24576, 2048).bitcast(BF16).rearrange("p (j o) -> p j o", j=IBC)
        zero = part(26624, 512)
        xnB = part(0, 2048).rearrange("p (t c) -> p t c", t=TPB)
        xnBT = part(2048, 1024).rearrange("p (s c) -> p s c", s=2)
        magB = part(3072, 2048).rearrange("p (s c) -> p s c", s=2)
        intB = part(5120, 1024).bitcast(BF16).rearrange("p (s c) -> p s c", s=2)
        qBT = part(6144, 1024).bitcast(BF16).rearrange("p (j t) -> p j t", j=DC)
        sqB = part(7168, 4096).rearrange("p (k t) -> p k t", k=IBC)
        reluB = part(11264, 1024).rearrange("p (s c) -> p s c", s=2)
        q2T = part(12288, 1024).bitcast(BF16).rearrange("p (s k t) -> p s k t", s=2, k=IBC)
        ctT = part(13312, 1024).rearrange("p (k n) -> p k n", k=CC)
        wqk = part(14336, 512).rearrange("p (w k d) -> p w k d", w=2, k=CC)
        qk = part(14848, 1024).rearrange("p (w n) -> p w n", w=2)
        prob = part(15872, 2048).rearrange("p (t n) -> p t n", t=TPB)
        probT = part(17920, 2048).rearrange("p (j n) -> p j n", j=TPB)
        xnC = part(0, 2048).rearrange("p (t c) -> p t c", t=TPB)
        xnCT = part(2048, 2048).rearrange("p (j n) -> p j n", j=DC)
        swg = part(0, DC * FS).rearrange("p (j f) -> p j f", j=DC)
        swu = part(DC * FS, DC * FS).rearrange("p (j f) -> p j f", j=DC)
        swd = part(2 * DC * FS, FSC * D).rearrange("p (j h) -> p j h", j=FSC)
        hS = part(16896, FSC * SEQ).rearrange("p (j t) -> p j t", j=FSC)
        siluS = part(22528, 1024).rearrange("p (s c) -> p s c", s=2)
        normw = part(23552, 512)
        wrt = part(24064, DC * E).rearrange("p (j e) -> p j e", j=DC)
        wsg = part(24064 + DC * E, DC)
        xnD = part(24200, 2048).rearrange("p (t c) -> p t c", t=TPB)
        rt = [part(16896 + 512 * i, 512).rearrange("p (t e) -> p t e", e=E) for i in range(11)]
        top_v = part(24200, NT * 8).rearrange("p (t k) -> p t k", k=8)
        top_i = part(24328, NT * 8).bitcast(U32).rearrange("p (t k) -> p t k", k=8)
        top_f = part(24456, NT * 8).rearrange("p (t k) -> p t k", k=8)
        rcol = [part(24584 + NT * TOPK * i, NT * TOPK).rearrange("p (t k) -> p t k", k=TOPK) for i in range(8)]
        ewg = [part(4352 * s, 1408).rearrange("p (j f) -> p j f", j=DC) for s in range(2)]
        ewu = [part(4352 * s + 1408, 1408).rearrange("p (j f) -> p j f", j=DC) for s in range(2)]
        ewd = [part(4352 * s + 2816, 1536).rearrange("p (j h) -> p j h", j=3) for s in range(2)]
        erow = [part(8704 + 1024 * s, 1024).rearrange("p (c h) -> p c h", c=2) for s in range(2)]
        erT = [part(10752 + 1024 * s, 1024).rearrange("p (j t) -> p j t", j=DC) for s in range(2)]
        eh = part(12800, 768).rearrange("p (j t) -> p j t", j=3)
        esilu = part(13568, 768).rearrange("p (j t) -> p j t", j=3)
        ey = [part(14336 + 1024 * s, 1024).rearrange("p (c h) -> p c h", c=2) for s in range(2)]
        grow = [part(512 * s, 512) for s in range(4)]

        block = stack.enter_context(nc.Block())

        @block.sync
        def _(sp):
            sp.dma_start(tab[:, :], const_tab).then_inc(const_in, 16)
            sp.dma_start(gates[:, 0:2], g_xattn.partition_broadcast(P)).then_inc(const_in, 16)
            sp.dma_start(gates[:, 2:4], g_ffn.partition_broadcast(P)).then_inc(const_in, 16)
            sp.dma_start(bias_qk[:, 0:1], bq.rearrange("(p a) -> p a", a=1)).then_inc(const_in, 16)
            sp.dma_start(bias_qk[:, 1:2], bk.rearrange("(p a) -> p a", a=1)).then_inc(const_in, 16)
            sp.dma_start(X[:, :].rearrange("p (n c) -> p n c", c=D),
                         x.rearrange("b (t p) c -> p (b t) c", p=P)).then_inc(x_in, 16)
            for b in range(2):
                sp.dma_start(fs_buf[b], fside[b].rearrange("(t p) c -> p t c", p=P)).then_inc(fside_in[b], 16)
                sp.dma_start(cx_buf[b], ctx[b].rearrange("(t p) c -> p t c", p=P)).then_inc(ctx_in[b], 16)
            sp.dma_start(wupR.rearrange("p (j o) -> p j o", j=DC),
                         wupT.rearrange("(j p) o -> p j o", p=P)).then_inc(wb_in, 16)
            sp.dma_start(wdownR.rearrange("p (j o) -> p j o", j=IBC),
                         wdownT.rearrange("(j p) o -> p j o", p=P)).then_inc(wb_in, 16)
            sp.dma_start(had, const_had).then_inc(had_in, 16)
            for b in range(2, BATCH):
                sp.wait_ge(a_used, b - 1)
                sp.dma_start(fs_buf[b % 2], fside[b].rearrange("(t p) c -> p t c", p=P)).then_inc(fside_in[b % 2], 16)
                sp.dma_start(cx_buf[b % 2], ctx[b].rearrange("(t p) c -> p t c", p=P)).then_inc(ctx_in[b % 2], 16)
            sp.wait_ge(zeroed, 1)
            sp.dma_start(dispatched[0:SLOTS, :].rearrange("(n p) c -> p n c", p=P),
                         zero.unsqueeze(1).to_broadcast([P, SLOTS // P, D])).then_inc(rows_cleared, 16)
            sp.wait_ge(a_used, BATCH)
            sp.dma_start(wqk[:, 0, :, :], WqT.rearrange("(k p) d -> p k d", p=P)).then_inc(wc_in, 16)
            sp.dma_start(wqk[:, 1, :, :], WkT.rearrange("(k p) d -> p k d", p=P)).then_inc(wc_in, 16)
            for b in range(BATCH):
                if b:
                    sp.wait_ge(c_proj, 2 * b)
                sp.dma_start(ctT, ctxT[b].rearrange("(k p) n -> p k n", p=P)).then_inc(ctxT_in, 16)
            sp.wait_ge(b_done, NT)
            sp.dma_start(normw, w_norm.partition_broadcast(P)).then_inc(router_in, 16)
            sp.dma_start(wrt, w_router.rearrange("(j p) e -> p j e", p=P)).then_inc(router_in, 16)
            sp.dma_start(wsg, w_sgate.rearrange("(j p) a -> p (j a)", p=P),
                         allow_slow_non_contiguous=True).then_inc(router_in, 16)
            sp.wait_ge(c_done, NT)
            sp.dma_start(swg, sw_gate.rearrange("(j p) f -> p j f", p=P)).then_inc(shared_in, 16)
            sp.dma_start(swu, sw_up.rearrange("(j p) f -> p j f", p=P)).then_inc(shared_in, 16)
            sp.dma_start(swd, sw_down.rearrange("(j p) h -> p j h", p=P)).then_inc(shared_in, 16)

            def load_expert(e, s):
                sp.dma_start(ewg[s], w_gate[bass.ds(e, 1), :, :].rearrange("a (j p) f -> p (a j) f", p=P)).then_inc(ew_in[s], 16)
                sp.dma_start(ewu[s], w_up[bass.ds(e, 1), :, :].rearrange("a (j p) f -> p (a j) f", p=P)).then_inc(ew_in[s], 16)
                sp.dma_start(ewd[s][:, 0:2, :],
                             w_down[bass.ds(e, 1), 0:256, :].rearrange("a (j p) h -> p (a j) h", p=P)).then_inc(ew_in[s], 16)
                sp.dma_start(ewd[s][0:96, 2, :],
                             w_down[bass.ds(e, 1), 256:F, :].rearrange("a p h -> p (a h)")).then_inc(ew_in[s], 16)
                sp.dma_start(erow[s], dispatched[bass.ds(e * CAP, CAP), :].rearrange("(c p) h -> p c h", p=P)).then_inc(ew_in[s], 16)

            def store_expert(e, s):
                wait(sp, "sp", e_y, 2 * e + 4)
                sp.dma_start(expert_out[bass.ds(e * CAP, CAP), :].rearrange("(c p) h -> p c h", p=P), ey[s]).then_inc(y_out[s], 16)

            sp.wait_ge(s_added, NT + TPB)
            sp.wait_ge(scattered, 16 * NT * TOPK)
            load_expert(0, 0)
            load_expert(1, 1)
            with sp.Fori(0, E // 2 - 1) as i:
                for s in range(2):
                    wait(sp, "sp", e_down, 2 * (2 * i + s) + 2)
                    load_expert(2 * i + s + 2, s)
                    store_expert(2 * i + s, s)
            for s in range(2):
                store_expert(E - 2 + s, s)
            for T in range(NT):
                sp.wait_ge(combined, TOPK * (T + 1))
                sp.dma_start(out[T // TPB, (T % TPB) * P:(T % TPB + 1) * P, :], xtile(T)).then_inc(final_out, 16)
            sp.wait_ge(final_out, 16 * NT)

        @block.gpsimd
        def _(pool):
            pool.memset(zero, 0.0).then_inc(zeroed, 1)
            pool.memset(phalf, 0.5).then_inc(zeroed, 1)
            pool.memset(mhalf4, -0.5).then_inc(zeroed, 1)
            pool.wait_ge(zeroed, 3)

            def invroot(seq):
                wait(pool, "pool", var_ready, seq + 1)
                pool.tensor_tensor(rstd, veps, mhalf4, ALU.pow).then_inc(root_ready, 1)

            with pool.Fori(0, BATCH) as b:
                invroot(b)
                for r in range(2):
                    n = DC if r == 0 else CC
                    wait(pool, "pool", q_ratio, 2 * b + r + 1)
                    pool.tensor_tensor(root[:, 0:n], ratio[:, 0:n], phalf[:, 0:n], ALU.pow).then_inc(q_root, 1)
            with pool.Fori(0, BATCH) as b:
                invroot(BATCH + b)
                for c in range(IBC):
                    wait(pool, "pool", b_relu, IBC * b + c + 1)
                    pool.tensor_tensor(sqB[:, c, :], reluB[:, c % 2, :], reluB[:, c % 2, :], ALU.mult).then_inc(b_sq, 1)
            with pool.Fori(0, BATCH) as b:
                invroot(2 * BATCH + b)
            with pool.Fori(0, BATCH) as b:
                invroot(3 * BATCH + b)
                wait(pool, "pool", ms_ready, b + 1)
                pool.tensor_tensor(rms, ms, mhalf4, ALU.pow).then_inc(rms_ready, 1)
            pool.wait_ge(r_index, 1)
            pool.wait_ge(rows_cleared, 16)
            for T in range(NT):
                for k in range(TOPK):
                    c = T * TOPK + k
                    pool.indirect_dma_start(
                        out=dispatched, out_offset=bass.IndirectOffsetOnAxis(ap=scatter_at[:, c:c + 1], axis=0),
                        in_=XR[:, T * D:(T + 1) * D], in_offset=None).then_inc(scattered, 16)
            pool.wait_ge(y_out[0], 16 * (E // 2) + 16)
            pool.wait_ge(y_out[1], 16 * (E // 2) + 16)
            for T in range(NT):
                for k in range(TOPK):
                    c = T * TOPK + k
                    if c >= 4:
                        pool.wait_ge(combined, c - 3)
                    pool.indirect_dma_start(
                        out=grow[c % 4], out_offset=None, in_=expert_out,
                        in_offset=bass.IndirectOffsetOnAxis(ap=gather_at[:, c:c + 1], axis=0)).then_inc(gathered[c % 4], 16)

        @block.scalar
        def _(act):
            act.wait_ge(const_in, 80)
            act.activation(tg[:, 0:1], gates[:, 0:1], ACT.Tanh)
            act.activation(tg[:, 2:3], gates[:, 1:2], ACT.Tanh)
            act.activation(tg[:, 1:2], gates[:, 2:3], ACT.Tanh)
            act.activation(tg[:, 3:4], gates[:, 3:4], ACT.Tanh).then_inc(tanh_ready, 1)

            with act.Fori(0, BATCH) as b:
                for r in range(2):
                    C = D if r == 0 else CTX
                    nk = C // P
                    q = 2 * b + r
                    for t in range(8):
                        wait(act, "act", q_inv, 2 * q + t // 4 + 1)
                        act.activation(scaled[:, t, 0:C], scaled[:, t, 0:C], ACT.Identity, bias=magic,
                                       scale=rowinv[:, t:t + 1]).then_inc(q_magic, 1)
                    for t in range(8):
                        wait(act, "act", q_intT, 8 * q + t + 1)
                        act.activation(intsT[:, 0:nk, t * P:(t + 1) * P],
                                       bankb[4 + t % 2][:, 0:C].rearrange("p (j t) -> p j t", j=nk),
                                       ACT.Copy).then_inc(q_lhs, 1)
                    if r == 0:
                        for t in range(TPB):
                            wait(act, "act", a_h, TPB * b + t + 1)
                            act.activation(actA[:, t, :], hA[:, t, 0:IA], ACT.Silu).then_inc(a_silu, 1)
            with act.Fori(0, BATCH) as b:
                for t in range(TPB):
                    n = TPB * b + t
                    wait(act, "act", b_xnT, n + 1)
                    act.activation(xnBT[:, t % 2, :], bank[t % 2][:, :], ACT.Copy).then_inc(b_xnTs, 1)
                    wait(act, "act", b_inv, 2 * TPB * b + t + 1)
                    act.activation(magB[:, t % 2, 0:D], bank[2 + t % 2][:, :], ACT.Identity, bias=magic,
                                   scale=bs[:, 8 * t + 1:8 * t + 2]).then_inc(b_magic, 1)
                    wait(act, "act", b_intT, 2 * TPB * b + t + 1)
                    act.activation(qBT[:, :, t * P:(t + 1) * P],
                                   bankb[4 + t % 2][:, 0:D].rearrange("p (j t) -> p j t", j=DC),
                                   ACT.Copy).then_inc(b_q, 1)
                for c in range(IBC):
                    wait(act, "act", b_up, IBC * b + c + 1)
                    if c >= 2:
                        wait(act, "act", b_sq, IBC * b + c - 1)
                    act.activation(reluB[:, c % 2, :], bank[6 + c % 2][:, :], ACT.Relu).then_inc(b_relu, 1)
                for t in range(TPB):
                    n2 = 2 * TPB * b + TPB + t
                    wait(act, "act", b_inv, n2 + 1)
                    for h in range(2):
                        last = act.activation(magB[:, t % 2, h * 512:(h + 1) * 512], bank[2 * (t % 2) + h][:, :],
                                              ACT.Identity, bias=magic, scale=bs[:, 8 * t + 4:8 * t + 5])
                    last.then_inc(b_magic, 1)
                    wait(act, "act", b_intT, n2 + 1)
                    act.activation(q2T[:, t % 2, :, :],
                                   bankb[4 + t % 2][:, :].rearrange("p (k t) -> p k t", k=IBC),
                                   ACT.Copy).then_inc(b_q, 1)
            with act.Fori(0, BATCH) as b:
                for w in range(2):
                    wait(act, "act", c_proj, 2 * b + w + 1)
                    act.activation(qk[:, w, :], bank[w][:, :], ACT.Identity, bias=bias_qk[:, w:w + 1],
                                   scale=1.0).then_inc(c_qk, 1)
                for t in range(TPB):
                    wait(act, "act", c_max, TPB * b + t + 1)
                    act.activation(prob[:, t, :], bank[2 + t][:, :], ACT.Exp, bias=negmax[:, t:t + 1], scale=1.0,
                                   accum_out=esum[:, t:t + 1]).then_inc(c_exp, 1)
                for t in range(TPB):
                    wait(act, "act", c_probT, TPB * b + t + 1)
                    act.activation(probT[:, :, t * P:(t + 1) * P],
                                   bank[6 + t % 2][:, :].rearrange("p (j t) -> p j t", j=TPB), ACT.Copy).then_inc(c_pT, 1)
                for t in range(TPB):
                    wait(act, "act", c_xnT, TPB * b + t + 1)
                    act.activation(xnCT[:, :, t * P:(t + 1) * P],
                                   bank[t % 2][:, :].rearrange("p (j t) -> p j t", j=DC), ACT.Copy).then_inc(c_xT, 1)
            with act.Fori(0, BATCH) as b:
                for t in range(TPB):
                    wait(act, "act", d_xrT, TPB * b + t + 1)
                    act.activation(XRT[:, :, bass.ds((TPB * b + t) * P, P)],
                                   bank[t % 2][:, :].rearrange("p (j t) -> p j t", j=DC), ACT.Copy).then_inc(d_xT, 1)
            act.wait_ge(d_logit, 1)
            act.activation(sg_e, bank[3][:, 0:NT], ACT.Exp, scale=-1.0).then_inc(r_exp, 1)
            act.wait_ge(r_shift, 1)
            act.activation(rt[1], rt[0], ACT.Exp).then_inc(r_exp, 1)
            with act.Fori(0, BATCH) as b:
                for c in range(FSC):
                    wait(act, "act", s_gu, FSC * b + c + 1)
                    wait(act, "act", s_h, FSC * b + c + 1)
                    act.activation(siluS[:, c % 2, :], bank[4 + 2 * (c % 2)][:, :], ACT.Silu).then_inc(s_silu, 1)
            def expert_act(e, s):
                for h in range(2):
                    wait(act, "act", e_rowsT, 2 * e + h + 1)
                    act.activation(erT[s][:, 2 * h:2 * h + 2, :],
                                   bank[h][:, :].rearrange("p (j t) -> p j t", j=2), ACT.Copy).then_inc(e_xT, 1)

            def expert_silu(e, s):
                for c, (f0, fn) in enumerate(FCH):
                    wait(act, "act", e_gu, 3 * e + c + 1)
                    act.activation(esilu[0:fn, c, :], bank[2 + c][0:fn, 0:CAP], ACT.Silu).then_inc(e_silu, 1)

            expert_act(0, 0)
            with act.Fori(0, E // 2 - 1) as i:
                for s in range(2):
                    expert_silu(2 * i + s, s)
                    expert_act(2 * i + s + 1, 1 - s)
            expert_silu(E - 2, 0)
            expert_act(E - 1, 1)
            expert_silu(E - 1, 1)

        @block.tensor
        def _(pe):
            pe.wait_ge(const_in, 80)
            pe.wait_ge(ident_ready, 1)

            def spread(dst, col, n):
                for j in range(n):
                    last = pe.matmul(dst[:, j * P:(j + 1) * P], col[:, j:j + 1].to_broadcast([P, P]), ident,
                                     start=True, stop=True)
                return last

            with pe.Fori(0, BATCH) as b:
                for r in range(2):
                    C = D if r == 0 else CTX
                    nk = C // P
                    q = 2 * b + r
                    for w in range(2):
                        wait(pe, "pe", q_fold, 2 * q + w + 1)
                        for j in range(nk):
                            last = pe.transpose(bank[w][:, j * P:(j + 1) * P], fold[:, w, 2, j * P:(j + 1) * P], ident)
                        last.then_inc(q_foldT, 1)
                    wait(pe, "pe", q_s, q + 1)
                    spread(bank[2], rs_col, nk).then_inc(q_bc, 1)
                    spread(bank[3], s_col, nk).then_inc(q_bc, 1)
                    for t in range(8):
                        wait(pe, "pe", q_int, 8 * q + t + 1)
                        if t >= 2:
                            wait(pe, "pe", q_lhs, 8 * q + t - 1)
                        for j in range(nk):
                            last = pe.transpose(bankb[4 + t % 2][:, j * P:(j + 1) * P], ints[:, t, j * P:(j + 1) * P],
                                                identb[:, :])
                        last.then_inc(q_intT, 1)
                    spread(bank[3], rowscale[:, 4:8], TPB).then_inc(q_wbc, 1)
                    wait(pe, "pe", q_lhs, 8 * q + 8)
                    for t in range(TPB):
                        if t >= 2:
                            wait(pe, "pe", a_h if r == 0 else a_out, TPB * b + t - 1)
                        for j in range(nk):
                            last = pe.matmul(bank[6 + t % 2][:, :], intsT[:, j, t * P:(t + 1) * P],
                                             intsT[:, j, SEQ:2 * SEQ], start=(j == 0), stop=(j == nk - 1))
                        last.then_inc(q_mm, 1)
            pe.wait_ge(wb_sum, 1)
            pe.matmul(bank[0][:, 0:2], ones, wsum, start=True, stop=True).then_inc(wb_tot, 1)
            pe.wait_ge(had_in, 16)
            pe.wait_ge(wb_sum, 2)
            with pe.Fori(0, BATCH) as b:
                for t in range(TPB):
                    wait(pe, "pe", b_xn, TPB * b + t + 1)
                    for j in range(DC):
                        last = pe.transpose(bank[t % 2][:, j * P:(j + 1) * P], xnB[:, t, j * P:(j + 1) * P], ident)
                    last.then_inc(b_xnT, 1)
                    wait(pe, "pe", b_xnTs, TPB * b + t + 1)
                    for j in range(DC):
                        last = pe.matmul(bank[2 + t % 2][:, :], xnBT[:, t % 2, j * P:(j + 1) * P],
                                         had[:, j * IB:j * IB + D], start=(j == 0), stop=(j == DC - 1))
                    last.then_inc(b_rot, 1)
                    wait(pe, "pe", b_int, 2 * TPB * b + t + 1)
                    for j in range(DC):
                        last = pe.transpose(bankb[4 + t % 2][:, j * P:(j + 1) * P], intB[:, t % 2, j * P:(j + 1) * P],
                                            identb[:, :])
                    last.then_inc(b_intT, 1)
                wait(pe, "pe", b_q, 2 * TPB * b + TPB)
                for c in range(IBC):
                    if c >= 2:
                        wait(pe, "pe", b_relu, IBC * b + c - 1)
                    for j in range(DC):
                        last = pe.matmul(bank[6 + c % 2][:, :], wupQ[:, j, c * P:(c + 1) * P], qBT[:, j, :],
                                         start=(j == 0), stop=(j == DC - 1))
                    last.then_inc(b_up, 1)
                wait(pe, "pe", b_sq, IBC * (b + 1))
                for t in range(TPB):
                    for h in range(2):
                        for k in range(IBC):
                            last = pe.matmul(bank[2 * (t % 2) + h][:, :], sqB[:, k, t * P:(t + 1) * P],
                                             had[:, k * IB + h * 512:k * IB + (h + 1) * 512],
                                             start=(k == 0), stop=(k == IBC - 1))
                    last.then_inc(b_rot, 1)
                    wait(pe, "pe", b_int, 2 * TPB * b + TPB + t + 1)
                    for k in range(IBC):
                        last = pe.transpose(bankb[4 + t % 2][:, k * P:(k + 1) * P], intB[:, t % 2, k * P:(k + 1) * P],
                                            identb[:, :])
                    last.then_inc(b_intT, 1)
                    wait(pe, "pe", b_q, 2 * TPB * b + TPB + t + 1)
                    for k in range(IBC):
                        last = pe.matmul(bank[6 + t % 2][:, :], q2T[:, t % 2, k, :], wdownQ[:, k, :],
                                         start=(k == 0), stop=(k == IBC - 1))
                    last.then_inc(b_down, 1)
            pe.wait_ge(b_done, NT)
            pe.wait_ge(wc_in, 32)
            with pe.Fori(0, BATCH) as b:
                wait(pe, "pe", ctxT_in, 16 * b + 16)
                for w in range(2):
                    for k in range(CC):
                        last = pe.matmul(bank[w][:, :], wqk[:, w, k, :], ctT[:, k, :], start=(k == 0), stop=(k == CC - 1))
                    last.then_inc(c_proj, 1)
                wait(pe, "pe", c_qk, 2 * b + 2)
                for t in range(TPB):
                    pe.matmul(bank[2 + t][:, :], qk[:, 0, t * P:(t + 1) * P], qk[:, 1, :],
                              start=True, stop=True).then_inc(c_energy, 1)
                for t in range(TPB):
                    wait(pe, "pe", c_prob, TPB * b + t + 1)
                    if t >= 2:
                        wait(pe, "pe", c_pT, TPB * b + t - 1)
                    for j in range(TPB):
                        last = pe.transpose(bank[6 + t % 2][:, j * P:(j + 1) * P], prob[:, t, j * P:(j + 1) * P], ident)
                    last.then_inc(c_probT, 1)
                for t in range(TPB):
                    wait(pe, "pe", c_xn, TPB * b + t + 1)
                    if t >= 2:
                        wait(pe, "pe", c_xT, TPB * b + t - 1)
                    for j in range(DC):
                        last = pe.transpose(bank[t % 2][:, j * P:(j + 1) * P], xnC[:, t, j * P:(j + 1) * P], ident)
                    last.then_inc(c_xnT, 1)
                wait(pe, "pe", c_pT, TPB * (b + 1))
                wait(pe, "pe", c_xT, TPB * (b + 1))
                for t in range(TPB):
                    for j in range(DC):
                        last = pe.matmul(bank[2 + t][:, :], xnCT[:, j, t * P:(t + 1) * P], probT[:, j, :],
                                         start=(j == 0), stop=(j == DC - 1))
                    last.then_inc(c_mix, 1)
                wait(pe, "pe", c_done, TPB * (b + 1))
            for b in range(BATCH):
                for t in range(TPB):
                    T = TPB * b + t
                    pe.wait_ge(d_xr, T + 1)
                    if T >= 2:
                        pe.wait_ge(d_xT, T - 1)
                    for j in range(DC):
                        last = pe.transpose(bank[t % 2][:, j * P:(j + 1) * P],
                                            XR[:, T * D + j * P:T * D + (j + 1) * P], ident)
                    last.then_inc(d_xrT, 1)
            pe.wait_ge(d_xT, NT)
            pe.wait_ge(router_in, 48)
            for T in range(NT):
                for j in range(DC):
                    pe.matmul(bank[2][:, T * E:(T + 1) * E], XRT[:, j, T * P:(T + 1) * P], wrt[:, j, :],
                              start=(j == 0), stop=(j == DC - 1))
                for j in range(DC):
                    last = pe.matmul(bank[3][:, T:T + 1], XRT[:, j, T * P:(T + 1) * P], wsg[:, j:j + 1],
                                     start=(j == 0), stop=(j == DC - 1))
            last.then_inc(d_logit, 1)
            pe.wait_ge(r_mask, 1)
            pe.matmul(bank[0][:, :], tri, rt[7].rearrange("p t e -> p (t e)"), start=True, stop=True)
            pe.matmul(bank[1][:, :], ones, rt[7].rearrange("p t e -> p (t e)"), start=True, stop=True).then_inc(r_rank, 1)
            pe.wait_ge(shared_in, 48)
            pe.wait_ge(r_index, 1)
            with pe.Fori(0, BATCH) as b:
                for c in range(FSC):
                    wait(pe, "pe", s_h, FSC * b + c + 1)
                    for w, wt in enumerate((swg, swu)):
                        for j in range(DC):
                            last = pe.matmul(bank[4 + 2 * (c % 2) + w][:, :], wt[:, j, c * P:(c + 1) * P],
                                             XRT[:, j, bass.ds(b * SEQ, SEQ)], start=(j == 0), stop=(j == DC - 1))
                    last.then_inc(s_gu, 1)
                wait(pe, "pe", s_h, FSC * (b + 1) + 2)
                for t in range(TPB):
                    wait(pe, "pe", s_added, TPB * b + t + 1)
                    for c in range(FSC):
                        last = pe.matmul(bank[t][:, :], hS[:, c, t * P:(t + 1) * P], swd[:, c, :],
                                         start=(c == 0), stop=(c == FSC - 1))
                    last.then_inc(s_out, 1)

            def rows_transpose(s):
                for h in range(2):
                    for jj in range(2):
                        for c in range(2):
                            j = 2 * h + jj
                            last = pe.transpose(bank[h][:, jj * CAP + c * P:jj * CAP + (c + 1) * P],
                                                erow[s][:, c, j * P:(j + 1) * P], ident)
                    last.then_inc(e_rowsT, 1)

            def gate_up(e, s):
                wait(pe, "pe", e_xT, 2 * e + 2)
                for c, (f0, fn) in enumerate(FCH):
                    wait(pe, "pe", e_h, 3 * e + c + 1)
                    for w, wt in enumerate((ewg[s], ewu[s])):
                        for j in range(DC):
                            last = pe.matmul(bank[2 + c][0:fn, w * CAP:(w + 1) * CAP], wt[:, j, f0:f0 + fn],
                                             erT[s][:, j, :], start=(j == 0), stop=(j == DC - 1))
                    last.then_inc(e_gu, 1)

            def down(e, s):
                wait(pe, "pe", e_h, 3 * e + 3 + 3)
                for t in range(2):
                    wait(pe, "pe", e_y, 2 * e + t + 1)
                    for c, (f0, fn) in enumerate(FCH):
                        last = pe.matmul(bank[5 + t][:, :], eh[0:fn, c, t * P:(t + 1) * P], ewd[s][0:fn, c, :],
                                         start=(c == 0), stop=(c == 2))
                    last.then_inc(e_down, 1)

            pe.wait_ge(s_added, NT + TPB)
            pe.wait_ge(ew_in[0], 80)
            rows_transpose(0)
            with pe.Fori(0, E // 2 - 1) as i:
                gate_up(2 * i, 0)
                wait(pe, "pe", ew_in[1], 80 * i + 80)
                rows_transpose(1)
                down(2 * i, 0)
                gate_up(2 * i + 1, 1)
                wait(pe, "pe", ew_in[0], 80 * i + 160)
                rows_transpose(0)
                down(2 * i + 1, 1)
            gate_up(E - 2, 0)
            pe.wait_ge(ew_in[1], 80 * (E // 2))
            rows_transpose(1)
            down(E - 2, 0)
            gate_up(E - 1, 1)
            down(E - 1, 1)

        @block.vector
        def _(dve):
            dve.wait_ge(const_in, 80)
            dve.tensor_copy(identb[:, :], ident).then_inc(ident_ready, 1)
            dve.sem_inc(s_h, 2)
            dve.sem_inc(e_h, 3)
            dve.sem_inc(s_added, TPB)
            dve.sem_inc(e_y, 2)
            for s in range(2):
                dve.sem_inc(y_out[s], 16)
            dve.wait_ge(tanh_ready, 1)
            dve.wait_ge(x_in, 16)

            def layernorm(seq, b, dst, signal):
                for t in range(TPB):
                    dve.bn_stats(bn[:, 6 * t:6 * t + 6], xtile(TPB * b + t))
                dve.drain()
                for t in range(TPB):
                    dve.bn_aggr(mv[:, 2 * t:2 * t + 2], bn[:, 6 * t:6 * t + 6])
                dve.drain()
                dve.tensor_scalar(veps, mv.rearrange("p (t k) -> p t k", k=2)[:, :, 1], 1e-5, None,
                                  ALU.add).then_inc(var_ready, 1)
                wait(dve, "dve", root_ready, seq + 1)
                for t in range(TPB):
                    last = dve.tensor_scalar(dst[:, t, :], xtile(TPB * b + t), mv[:, 2 * t:2 * t + 1],
                                             rstd[:, t:t + 1], ALU.subtract, ALU.mult)
                    if signal is not None:
                        last.then_inc(signal, 1)
                dve.drain()

            def quantise(q, C, src, wsrc):
                nk = C // P
                for w, s in enumerate((src, wsrc)):
                    dve.tensor_reduce(fold[:, w, 2, 0:C], s.rearrange("p t c -> p c t"), AX.X, ALU.max,
                                      apply_absolute_value=True).then_inc(q_fold, 1)
                for w in range(2):
                    wait(dve, "dve", q_foldT, 2 * q + w + 1)
                    dve.tensor_reduce(maxs[:, 4 * w:4 * w + nk], bank[w][:, 0:C].rearrange("p (j t) -> p j t", j=nk),
                                      AX.X, ALU.max, apply_absolute_value=True)
                dve.drain()
                dve.tensor_scalar(lim[:, 0:nk], maxs[:, 0:nk], TINY, None, ALU.max)
                dve.tensor_scalar(lim[:, 4:4 + nk], maxs[:, 4:4 + nk], TINY, None, ALU.max)
                dve.drain()
                dve.reciprocal(maxs[:, 4:4 + nk], lim[:, 4:4 + nk])
                dve.drain()
                dve.tensor_tensor(ratio[:, 0:nk], lim[:, 0:nk], maxs[:, 4:4 + nk], ALU.mult).then_inc(q_ratio, 1)
                wait(dve, "dve", q_root, q + 1)
                dve.tensor_scalar(s_col[:, 0:nk], root[:, 0:nk], TINY, None, ALU.max)
                dve.drain()
                dve.reciprocal(rs_col[:, 0:nk], s_col[:, 0:nk]).then_inc(q_s, 1)
                for w, s in enumerate((src, wsrc)):
                    wait(dve, "dve", q_bc, 2 * q + w + 1)
                    for t in range(4):
                        dve.tensor_tensor(scaled[:, 4 * w + t, 0:C], s[:, t, :], bank[2 + w][:, 0:C], ALU.mult)
                    dve.drain()
                    dve.tensor_reduce(rowmax[:, 4 * w:4 * w + 4], scaled[:, 4 * w:4 * w + 4, 0:C], AX.X, ALU.max,
                                      apply_absolute_value=True)
                    dve.drain()
                    dve.tensor_scalar(rowscale[:, 4 * w:4 * w + 4], rowmax[:, 4 * w:4 * w + 4], TINY, 1.0 / 127.0,
                                      ALU.max, ALU.mult)
                    dve.drain()
                    dve.reciprocal(rowinv[:, 4 * w:4 * w + 4], rowscale[:, 4 * w:4 * w + 4]).then_inc(q_inv, 1)
                for t in range(8):
                    wait(dve, "dve", q_magic, 8 * q + t + 1)
                    dve.tensor_scalar(ints[:, t, 0:C], scaled[:, t, 0:C], MAGIC, None, ALU.subtract).then_inc(q_int, 1)
                dve.tensor_scalar(gscale, rowscale[:, 0:4], tg[:, 0:1], None, ALU.mult)
                wait(dve, "dve", q_wbc, q + 1)

            with dve.Fori(0, BATCH // 2) as pair:
                for half in range(2):
                    b = 2 * pair + half
                    layernorm(b, b, xnA, None)
                    wait(dve, "dve", fside_in[half], 16 * pair + 16)
                    quantise(2 * b, D, xnA, fs_buf[half])
                    for t in range(TPB):
                        wait(dve, "dve", q_mm, TPB * 2 * b + t + 1)
                        if t == 0:
                            dve.tensor_copy(scaled[:, 7, :], bank[3][:, :])
                            dve.drain()
                        dve.scalar_tensor_tensor(hA[:, t, :], bank[6 + t % 2][:, :], rowscale[:, t:t + 1],
                                                 scaled[:, 7, :], ALU.mult, ALU.mult).then_inc(a_h, 1)
                    for t in range(TPB):
                        wait(dve, "dve", a_silu, TPB * b + t + 1)
                        dve.tensor_tensor(actA[:, t, :], actA[:, t, :], hA[:, t, IA:2 * IA], ALU.mult)
                    dve.drain()
                    wait(dve, "dve", ctx_in[half], 16 * pair + 16)
                    quantise(2 * b + 1, CTX, actA, cx_buf[half])
                    for t in range(TPB):
                        wait(dve, "dve", q_mm, TPB * (2 * b + 1) + t + 1)
                        if t == 0:
                            dve.tensor_copy(scaled[:, 7, :], bank[3][:, :])
                            dve.drain()
                        dve.scalar_tensor_tensor(hA[:, t, :], bank[6 + t % 2][:, :], gscale[:, t:t + 1],
                                                 scaled[:, 7, :], ALU.mult, ALU.mult).then_inc(a_out, 1)
                        dve.drain()
                        last = dve.tensor_tensor(xtile(TPB * b + t), xtile(TPB * b + t), hA[:, t, :], ALU.add)
                    last.then_inc(a_used, 1)
                    dve.drain()
            dve.wait_ge(wb_in, 32)
            dve.tensor_reduce(wsum[:, 0:1], wupR, AX.X, ALU.add, apply_absolute_value=True)
            dve.tensor_reduce(wsum[:, 1:2], wdownR, AX.X, ALU.add, apply_absolute_value=True).then_inc(wb_sum, 1)
            dve.wait_ge(wb_tot, 1)
            dve.tensor_scalar(wscale, bank[0][:, 0:2], 1.0 / (IB * D), 1e-5, ALU.mult, ALU.max)
            dve.drain()
            dve.reciprocal(winv, wscale)
            dve.drain()
            for w, (raw, dst) in enumerate(((wupR, wupQ), (wdownR, wdownQ))):
                dve.tensor_scalar(raw, raw, winv[:, w:w + 1], MAGIC, ALU.mult, ALU.add)
                dve.drain()
                dve.tensor_scalar(raw, raw, MAGIC, 1.0, ALU.subtract, ALU.min)
                dve.drain()
                last = dve.tensor_scalar(dst.rearrange("p j o -> p (j o)"), raw, -1.0, None, ALU.max)
            last.then_inc(wb_sum, 1)
            c1 = float(D) ** -0.5
            c2 = float(IB) ** -0.5
            dve.drain()
            with dve.Fori(0, BATCH) as b:
                layernorm(BATCH + b, b, xnB, b_xn)
                for t in range(TPB):
                    v = bs[:, 8 * t:8 * t + 8]
                    wait(dve, "dve", b_rot, 2 * TPB * b + t + 1)
                    dve.tensor_reduce(v[:, 0:1], bank[2 + t % 2][:, :], AX.X, ALU.max, apply_absolute_value=True)
                    dve.drain()
                    dve.tensor_scalar(v[:, 0:1], v[:, 0:1], c1, 1e-5, ALU.mult, ALU.max)
                    dve.drain()
                    dve.reciprocal(v[:, 2:3], v[:, 0:1])
                    dve.drain()
                    dve.tensor_scalar(v[:, 1:2], v[:, 2:3], 127.0 * c1, None, ALU.mult).then_inc(b_inv, 1)
                    dve.tensor_scalar(v[:, 3:4], v[:, 0:1], 1.0 / 127.0, wscale[:, 0:1], ALU.mult, ALU.mult)
                    wait(dve, "dve", b_magic, 2 * TPB * b + t + 1)
                    dve.tensor_scalar(intB[:, t % 2, 0:D], magB[:, t % 2, 0:D], MAGIC, None, ALU.subtract).then_inc(b_int, 1)
                dve.drain()
                for t in range(TPB):
                    v = bs[:, 8 * t:8 * t + 8]
                    dve.tensor_scalar(v[:, 5:6], v[:, 3:4], v[:, 3:4], c2, ALU.mult, ALU.mult)
                    wait(dve, "dve", b_rot, 2 * TPB * b + TPB + t + 1)
                    for h in range(2):
                        dve.tensor_reduce(v[:, 6 + h:7 + h], bank[2 * (t % 2) + h][:, :], AX.X, ALU.max,
                                          apply_absolute_value=True)
                    dve.drain()
                    dve.tensor_tensor(v[:, 6:7], v[:, 6:7], v[:, 7:8], ALU.max)
                    dve.drain()
                    dve.tensor_scalar(v[:, 6:7], v[:, 6:7], v[:, 5:6], None, ALU.mult)
                    dve.drain()
                    dve.tensor_scalar(v[:, 6:7], v[:, 6:7], 1e-5, None, ALU.max)
                    dve.drain()
                    dve.reciprocal(v[:, 7:8], v[:, 6:7])
                    dve.drain()
                    dve.tensor_scalar(v[:, 4:5], v[:, 7:8], v[:, 5:6], 127.0, ALU.mult, ALU.mult).then_inc(b_inv, 1)
                    dve.tensor_scalar(v[:, 0:1], v[:, 6:7], 1.0 / 127.0, wscale[:, 1:2], ALU.mult, ALU.mult)
                    wait(dve, "dve", b_magic, 2 * TPB * b + TPB + t + 1)
                    dve.tensor_scalar(intB[:, t % 2, :], magB[:, t % 2, :], MAGIC, None, ALU.subtract).then_inc(b_int, 1)
                    dve.drain()
                    dve.tensor_scalar(v[:, 0:1], v[:, 0:1], tg[:, 1:2], None, ALU.mult)
                    dve.drain()
                    wait(dve, "dve", b_down, TPB * b + t + 1)
                    dve.scalar_tensor_tensor(xtile(TPB * b + t), bank[6 + t % 2][:, :], v[:, 0:1], xtile(TPB * b + t),
                                             ALU.mult, ALU.add).then_inc(b_done, 1)
                dve.drain()
            with dve.Fori(0, BATCH) as b:
                for t in range(TPB):
                    wait(dve, "dve", c_energy, TPB * b + t + 1)
                    dve.tensor_reduce(negmax[:, t:t + 1], bank[2 + t][:, :], AX.X, ALU.max, negate=True).then_inc(c_max, 1)
                for t in range(TPB):
                    wait(dve, "dve", c_exp, TPB * b + t + 1)
                    dve.reciprocal(ersum[:, t:t + 1], esum[:, t:t + 1])
                    dve.drain()
                    dve.tensor_scalar(prob[:, t, :], prob[:, t, :], ersum[:, t:t + 1], None, ALU.mult).then_inc(c_prob, 1)
                layernorm(2 * BATCH + b, b, xnC, c_xn)
                for t in range(TPB):
                    wait(dve, "dve", c_mix, TPB * b + t + 1)
                    dve.scalar_tensor_tensor(xtile(TPB * b + t), bank[2 + t][:, :], tg[:, 2:3], xtile(TPB * b + t),
                                             ALU.mult, ALU.add).then_inc(c_done, 1)
                dve.drain()
            dve.wait_ge(router_in, 48)
            with dve.Fori(0, BATCH) as b:
                layernorm(3 * BATCH + b, b, xnD, None)
                dve.tensor_tensor(ms, rstd, rstd, ALU.mult)
                dve.drain()
                dve.tensor_tensor(ms, ms, mv.rearrange("p (t k) -> p t k", k=2)[:, :, 1], ALU.mult)
                dve.drain()
                dve.tensor_scalar(ms, ms, 1e-6, None, ALU.add).then_inc(ms_ready, 1)
                wait(dve, "dve", rms_ready, b + 1)
                for t in range(TPB):
                    T = TPB * b + t
                    dve.scalar_tensor_tensor(XR[:, bass.ds(T * D, D)], xnD[:, t, :], rms[:, t:t + 1], normw,
                                             ALU.mult, ALU.mult).then_inc(d_xr, 1)
                    dve.scalar_tensor_tensor(xtile(T), xnD[:, t, :], tg[:, 3:4], xtile(T), ALU.mult, ALU.add)
                dve.drain()
            dve.wait_ge(d_logit, 1)
            logits = bank[2][:, :].rearrange("p (t e) -> p t e", e=E)

            def per_tile(v):
                return v.unsqueeze(2).to_broadcast([P, NT, E])

            dve.tensor_reduce(rmax, logits, AX.X, ALU.max)
            dve.drain()
            dve.tensor_tensor(rt[0], logits, per_tile(rmax), ALU.subtract).then_inc(r_shift, 1)
            dve.wait_ge(r_exp, 2)
            dve.tensor_reduce(rsum, rt[1], AX.X, ALU.add)
            dve.drain()
            dve.reciprocal(rmax, rsum)
            dve.tensor_scalar(sg_e, sg_e, 1.0, None, ALU.add)
            dve.drain()
            dve.reciprocal(sgate, sg_e)
            dve.tensor_tensor(rt[2], rt[1], per_tile(rmax), ALU.mult)
            dve.drain()
            dve.tensor_scalar(sgate, sgate, tg[:, 3:4], None, ALU.mult)
            for T in range(NT):
                dve.max(top_v[:, T, :], rt[2][:, T, :])
            dve.drain()
            for T in range(NT):
                dve.max_index(top_i[:, T, :], top_v[:, T, :], rt[2][:, T, :])
            dve.drain()
            dve.tensor_copy(top_f, top_i)
            dve.drain()
            iota_all = iota.unsqueeze(1).to_broadcast([P, NT, E])
            for k in range(TOPK):
                dve.tensor_tensor(rt[3 + k], iota_all, per_tile(top_f[:, :, k]), ALU.is_equal)
            dve.drain()
            dve.tensor_tensor(rt[7], rt[3], rt[4], ALU.add)
            dve.tensor_tensor(rt[8], rt[5], rt[6], ALU.add)
            dve.drain()
            dve.tensor_tensor(rt[7], rt[7], rt[8], ALU.add).then_inc(r_mask, 1)
            dve.wait_ge(r_rank, 1)
            totals = bank[1][:, :].rearrange("p (t e) -> p t e", e=E)
            dve.memset(rt[8][:, 0:1, :], 0.0)
            dve.tensor_copy(rt[8][:, 1:NT, :], totals[:, 0:NT - 1, :])
            dve.drain()
            a, o, step = 8, 9, 1
            while step < NT:
                dve.tensor_copy(rt[o][:, 0:step, :], rt[a][:, 0:step, :])
                dve.tensor_tensor(rt[o][:, step:NT, :], rt[a][:, step:NT, :], rt[a][:, 0:NT - step, :], ALU.add)
                dve.drain()
                a, o, step = o, a, 2 * step
            dve.tensor_tensor(rt[a], rt[a], bank[0][:, :].rearrange("p (t e) -> p t e", e=E), ALU.add)
            dve.drain()
            pos, ok, dest, low, trash, t0, kept_w = rcol[0:7]
            for k in range(TOPK):
                dve.tensor_tensor(rt[3 + k], rt[3 + k], rt[a], ALU.mult)
            dve.drain()
            for k in range(TOPK):
                dve.tensor_reduce(pos[:, :, k], rt[3 + k], AX.X, ALU.add)
            dve.drain()
            dve.tensor_scalar(ok, pos, float(CAP), None, ALU.is_lt)
            dve.tensor_scalar(low, pos, float(CAP - 1), None, ALU.min)
            dve.tensor_scalar(t0, top_f[:, :, 0:TOPK], float(CAP), None, ALU.mult)
            dve.drain()
            dve.tensor_tensor(dest, t0, pos, ALU.add)
            dve.tensor_tensor(low, t0, low, ALU.add)
            dve.tensor_tensor(kept_w, top_v[:, :, 0:TOPK], ok, ALU.mult)
            dve.drain()
            dve.tensor_scalar(choice_w.rearrange("p (t k) -> p t k", k=TOPK), kept_w, tg[:, 3:4], None, ALU.mult)
            dve.tensor_copy(trash, spare)
            dve.tensor_copy(gather_at.rearrange("p (t k) -> p t k", k=TOPK), low)
            dve.drain()
            dve.tensor_tensor(dest, dest, trash, ALU.subtract)
            dve.drain()
            dve.tensor_tensor(dest, dest, ok, ALU.mult)
            dve.drain()
            dve.tensor_tensor(dest, dest, trash, ALU.add)
            dve.drain()
            dve.tensor_copy(scatter_at.rearrange("p (t k) -> p t k", k=TOPK), dest)
            dve.drain()
            dve.sem_inc(r_index, 1)
            with dve.Fori(0, BATCH) as b:
                for c in range(FSC):
                    wait(dve, "dve", s_silu, FSC * b + c + 1)
                    dve.tensor_tensor(hS[:, c, :], siluS[:, c % 2, :], bank[5 + 2 * (c % 2)][:, :],
                                      ALU.mult).then_inc(s_h, 1)
                for t in range(TPB):
                    T = TPB * b + t
                    wait(dve, "dve", s_out, T + 1)
                    dve.scalar_tensor_tensor(xtile(T), bank[t][:, :], sgate[:, bass.ds(T, 1)], xtile(T),
                                             ALU.mult, ALU.add).then_inc(s_added, 1)

            with dve.Fori(0, E // 2) as i:
                for s in range(2):
                    e = 2 * i + s
                    for c, (f0, fn) in enumerate(FCH):
                        wait(dve, "dve", e_silu, 3 * e + c + 1)
                        dve.tensor_tensor(eh[0:fn, c, :], esilu[0:fn, c, :], bank[2 + c][0:fn, CAP:2 * CAP],
                                          ALU.mult).then_inc(e_h, 1)
                    wait(dve, "dve", y_out[s], 16 * i + 16)
                    for t in range(2):
                        wait(dve, "dve", e_down, 2 * e + t + 1)
                        dve.tensor_copy(ey[s][:, t, :], bank[5 + t][:, :]).then_inc(e_y, 1)
            for T in range(NT):
                for k in range(TOPK):
                    c = T * TOPK + k
                    dve.wait_ge(gathered[c % 4], 16 * (c // 4 + 1))
                    dve.scalar_tensor_tensor(xtile(T), grow[c % 4], choice_w[:, c:c + 1], xtile(T),
                                             ALU.mult, ALU.add).then_inc(combined, 1)
                    dve.drain()


_INS = ["x", "fside_BxS2xS2_0", "ctx_1024", "g_xattn", "g_ffn", "w_up_T", "w_down_T", "Wq_T", "L1_xattn_bq", "Wk_T",
        "L1_xattn_bk", "L1_ffn_w_norm", "L1_ffn_w_router", "L1_ffn_w_gate", "L1_ffn_w_up", "L1_ffn_w_down",
        "L1_ffn_sw_gate", "L1_ffn_sw_up", "L1_ffn_sw_down", "L1_ffn_w_shared_gate", "ctx_T", "const_tab", "const_had"]


def kernel(**inputs):
    import numpy as _np
    import concourse.bacc as _bacc
    from concourse import mybir as _mybir
    from concourse.bass_utils import run_bass_kernel_spmd as _run

    given = dict(inputs)
    given["w_up_T"] = _np.transpose(inputs["L0_ffn_w_up"])
    given["w_down_T"] = _np.transpose(inputs["L0_ffn_w_down"])
    given["Wq_T"] = _np.transpose(inputs["L1_xattn_Wq"])
    given["Wk_T"] = _np.transpose(inputs["L1_xattn_Wk"])
    given["ctx_T"] = _np.transpose(inputs["ctx_1024"], (0, 2, 1))
    p = _np.arange(P)
    tab = _np.zeros((P, TAB), _np.float32)
    tab[p, p] = 1.0
    tab[:, P:2 * P] = p[:, None] < p[None, :]
    tab[:, 2 * P:3 * P] = 1.0
    tab[:, 3 * P:3 * P + E] = _np.arange(E)
    tab[:, 3 * P + E] = MAGIC
    tab[:, 3 * P + E + 1:] = SLOTS + _np.arange(NT * TOPK)[None, :] * P + p[:, None]
    had = _np.ones((1, 1), _np.float32)
    while had.shape[0] < IB:
        had = _np.block([[had, had], [had, -had]])
    given["const_tab"] = tab
    given["const_had"] = _np.ascontiguousarray(had.reshape(IBC, P, IB).transpose(1, 0, 2)).reshape(P, IBC * IB)

    nc = _bacc.Bacc("TRN2", target_bir_lowering=False, num_devices=1)
    arrays, args = {}, []
    for name in _INS:
        a = _np.ascontiguousarray(given[name])
        arrays[f"in_{name}_dram"] = a
        args.append(nc.dram_tensor(f"in_{name}_dram", a.shape, _mybir.dt.from_np(a.dtype), kind="ExternalInput").ap())
    out = nc.dram_tensor("out_0_dram", (BATCH, SEQ, D), _mybir.dt.float32, kind="ExternalOutput").ap()
    flamingo_block(nc, *args, out)
    r = _run(nc, [arrays], core_ids=[0])
    return r.results[0]["out_0_dram"]
```
